# Optimizing a Trainium2 kernel written in Bass

```python
import numpy as np
import jax
import jax.numpy as jnp

def _softmax(x, axis=-1):
    return jax.nn.softmax(x, axis=axis)

def _gelu(x):
    return jax.nn.gelu(x, approximate=True)

def _silu(x):
    return jax.nn.silu(x)

def _sigmoid(x):
    return jax.nn.sigmoid(x)

def _layernorm(x, axis=-1, eps=1e-05):
    m = jnp.mean(x, axis=axis, keepdims=True)
    v = jnp.var(x, axis=axis, keepdims=True)
    return (x - m) / jnp.sqrt(v + eps)

def _scatter_add(tgt, idx, src, axis=0):
    return tgt.at[idx].add(src)

def _segment_sum(src, seg, n):
    return jax.ops.segment_sum(src, seg, n)
kernel_name = 'mk_recurrent_d2_jaxref_r8_7bb7ac'

def setup_inputs(seed: int=0):
    np.random.seed(seed)
    _w = jnp.asarray

    def _L0_attn_setup():
        import jax, jax.numpy as jnp
        import numpy as np
        ROPE_THETA = 10000.0
        N_HEAD = 16

        def _rope(x, theta):
            T, D = (x.shape[-2], x.shape[-1])
            pos = jnp.arange(T, dtype=jnp.float32)
            inv_freq = 1.0 / theta ** (jnp.arange(0, D, 2, dtype=jnp.float32) / D)
            freqs = pos[:, None] * inv_freq[None, :]
            cos = jnp.cos(freqs).astype(x.dtype)[None, None]
            sin = jnp.sin(freqs).astype(x.dtype)[None, None]
            x_even = x[..., ::2]
            x_odd = x[..., 1::2]
            rot = jnp.stack((x_even * cos - x_odd * sin, x_even * sin + x_odd * cos), axis=-1)
            return rot.reshape(x.shape)
        key = jax.random.key(seed)
        ks = jax.random.split(key, 5)
        B, T, E = (4, 256, 128)
        s = 0.02
        return {'x': jax.random.normal(ks[0], (B, T, E), jnp.float32), 'Wqkv': jax.random.normal(ks[1], (E, 3 * E), jnp.float32) * s, 'bqkv': jax.random.normal(ks[2], (3 * E,), jnp.float32) * s, 'Wproj': jax.random.normal(ks[3], (E, E), jnp.float32) * s, 'bproj': jax.random.normal(ks[4], (E,), jnp.float32) * s}
    _L0_attn_in = _L0_attn_setup()

    def _L0_ffn_setup():
        import jax, jax.numpy as jnp
        import numpy as np
        B, SEQ, DIM = (2, 512, 128)
        E, S = (8, 64)
        HID = 4 * DIM
        SCALE = DIM ** 0.5

        def rmsnorm(x, gamma):
            n = jnp.linalg.norm(x, axis=-1, keepdims=True)
            return x / jnp.maximum(n, 1e-12) * SCALE * gamma
        key = jax.random.key(seed)
        ks = jax.random.split(key, 4)
        w_init = lambda k, shape: jax.random.normal(k, shape, dtype=jnp.float32) * 0.02
        return {'x': jax.random.normal(ks[0], (B, SEQ, DIM), dtype=jnp.float32), 'norm_gamma': jnp.ones((DIM,), jnp.float32), 'slot_norm_gamma': jnp.ones((DIM,), jnp.float32), 'slot_embeds': jax.random.normal(ks[1], (E, S, DIM), dtype=jnp.float32), 'w1': w_init(ks[2], (E, DIM, HID)), 'b1': jnp.zeros((E, HID), jnp.float32), 'w2': w_init(ks[3], (E, HID, DIM)), 'b2': jnp.zeros((E, DIM), jnp.float32)}
    _L0_ffn_in = _L0_ffn_setup()

    def _L1_attn_setup():
        import jax, jax.numpy as jnp
        import numpy as np
        B, T, D, H = (2, 256, 128, 16)
        Dh = D // H

        def _rope(q, k):
            t = q.shape[2]
            dh = q.shape[3]
            inv_freq = 1.0 / 10000.0 ** (jnp.arange(0, dh, 2, dtype=jnp.float32) / dh)
            pos = jnp.arange(t, dtype=jnp.float32)
            freqs = pos[:, None] * inv_freq[None, :]
            sin = jnp.sin(freqs)[None, None]
            cos = jnp.cos(freqs)[None, None]

            def rot(x):
                xe, xo = (x[..., ::2], x[..., 1::2])
                re = xe * cos - xo * sin
                ro = xe * sin + xo * cos
                return jnp.stack([re, ro], axis=-1).reshape(x.shape)
            return (rot(q), rot(k))
        key = jax.random.key(seed)
        k1, k2, k3 = jax.random.split(key, 3)
        s = 1.0 / np.sqrt(D)
        return {'x': jax.random.normal(k1, (B, T, D), dtype=jnp.float32), 'w_qkv': jax.random.normal(k2, (3 * D, D), dtype=jnp.float32) * s, 'b_qkv': jnp.zeros((3 * D,), dtype=jnp.float32), 'w_out': jax.random.normal(k3, (D, D), dtype=jnp.float32) * s, 'b_out': jnp.zeros((D,), dtype=jnp.float32)}
    _L1_attn_in = _L1_attn_setup()

    def _L1_ffn_setup():
        import jax, jax.numpy as jnp
        import numpy as np
        N_EXPERTS = 16
        TOPK = 2
        CAPACITY_FACTOR = 1.0
        EPS_GATE = 1e-06
        LN_EPS = 1e-05
        key = jax.random.key(seed)
        ks = jax.random.split(key, 8)
        B, S, D, F, E = (4, 256, 128, 512, N_EXPERTS)
        Fp = F // E
        s = 0.02
        return {'x': jax.random.normal(ks[0], (B, S, D), dtype=jnp.float32), 'wg': s * jax.random.normal(ks[1], (D, E), dtype=jnp.float32), 'bg': jnp.zeros((E,), dtype=jnp.float32), 'w1': s * jax.random.normal(ks[2], (E, D, Fp), dtype=jnp.float32), 'b1': jnp.zeros((E, Fp), dtype=jnp.float32), 'w2': s * jax.random.normal(ks[3], (E, Fp, D), dtype=jnp.float32), 'b2': jnp.zeros((E, D), dtype=jnp.float32), 'gamma': jnp.ones((D,), dtype=jnp.float32), 'beta': jnp.zeros((D,), dtype=jnp.float32)}
    _L1_ffn_in = _L1_ffn_setup()
    _d = {'L0_attn_x': _L0_attn_in['x'], 'L0_attn_Wqkv': _L0_attn_in['Wqkv'], 'L0_attn_bqkv': _L0_attn_in['bqkv'], 'L0_attn_Wproj': _L0_attn_in['Wproj'], 'L0_attn_bproj': _L0_attn_in['bproj'], 'L0_ffn_norm_gamma': _L0_ffn_in['norm_gamma'], 'L0_ffn_slot_norm_gamma': _L0_ffn_in['slot_norm_gamma'], 'L0_ffn_slot_embeds': _L0_ffn_in['slot_embeds'], 'L0_ffn_w1': _L0_ffn_in['w1'], 'L0_ffn_b1': _L0_ffn_in['b1'], 'L0_ffn_w2': _L0_ffn_in['w2'], 'L0_ffn_b2': _L0_ffn_in['b2'], 'L1_attn_w_qkv': _L1_attn_in['w_qkv'], 'L1_attn_b_qkv': _L1_attn_in['b_qkv'], 'L1_attn_w_out': _L1_attn_in['w_out'], 'L1_attn_b_out': _L1_attn_in['b_out'], 'L1_ffn_wg': _L1_ffn_in['wg'], 'L1_ffn_bg': _L1_ffn_in['bg'], 'L1_ffn_w1': _L1_ffn_in['w1'], 'L1_ffn_b1': _L1_ffn_in['b1'], 'L1_ffn_w2': _L1_ffn_in['w2'], 'L1_ffn_b2': _L1_ffn_in['b2'], 'L1_ffn_gamma': _L1_ffn_in['gamma'], 'L1_ffn_beta': _L1_ffn_in['beta']}
    _x0 = _d['L0_attn_x']
    _d['L0_attn_x'] = jax.random.normal(jax.random.fold_in(jax.random.key(seed), 1), (2, 1024, 128), dtype=_x0.dtype)
    del _x0
    return _d

def reference(L0_attn_x, L0_attn_Wqkv, L0_attn_bqkv, L0_attn_Wproj, L0_attn_bproj, L0_ffn_norm_gamma, L0_ffn_slot_norm_gamma, L0_ffn_slot_embeds, L0_ffn_w1, L0_ffn_b1, L0_ffn_w2, L0_ffn_b2, L1_attn_w_qkv, L1_attn_b_qkv, L1_attn_w_out, L1_attn_b_out, L1_ffn_wg, L1_ffn_bg, L1_ffn_w1, L1_ffn_b1, L1_ffn_w2, L1_ffn_b2, L1_ffn_gamma, L1_ffn_beta):

    def _L0_attn_ref(x, Wqkv, bqkv, Wproj, bproj):
        import jax, jax.numpy as jnp
        import numpy as np
        ROPE_THETA = 10000.0
        N_HEAD = 16

        def _rope(x, theta):
            T, D = (x.shape[-2], x.shape[-1])
            pos = jnp.arange(T, dtype=jnp.float32)
            inv_freq = 1.0 / theta ** (jnp.arange(0, D, 2, dtype=jnp.float32) / D)
            freqs = pos[:, None] * inv_freq[None, :]
            cos = jnp.cos(freqs).astype(x.dtype)[None, None]
            sin = jnp.sin(freqs).astype(x.dtype)[None, None]
            x_even = x[..., ::2]
            x_odd = x[..., 1::2]
            rot = jnp.stack((x_even * cos - x_odd * sin, x_even * sin + x_odd * cos), axis=-1)
            return rot.reshape(x.shape)
        B, T, E = x.shape
        H = N_HEAD
        D = E // H
        qkv = x @ Wqkv + bqkv
        q, k, v = jnp.split(qkv, 3, axis=-1)
        q = q.reshape(B, T, H, D).transpose(0, 2, 1, 3)
        k = k.reshape(B, T, H, D).transpose(0, 2, 1, 3)
        v = v.reshape(B, T, H, D).transpose(0, 2, 1, 3)
        q = _rope(q, ROPE_THETA)
        k = _rope(k, ROPE_THETA)
        scores = jnp.einsum('bhqd,bhkd->bhqk', q, k) * D ** (-0.5)
        causal = jnp.tril(jnp.ones((T, T), dtype=bool))
        scores = jnp.where(causal[None, None], scores, -jnp.inf)
        weights = jax.nn.softmax(scores, axis=-1)
        out = jnp.einsum('bhqk,bhkd->bhqd', weights, v)
        out = out.transpose(0, 2, 1, 3).reshape(B, T, E)
        return out @ Wproj + bproj

    def _L0_ffn_ref(x, norm_gamma, slot_norm_gamma, slot_embeds, w1, b1, w2, b2):
        import jax, jax.numpy as jnp
        import numpy as np
        B, SEQ, DIM = (2, 512, 128)
        E, S = (8, 64)
        HID = 4 * DIM
        SCALE = DIM ** 0.5

        def rmsnorm(x, gamma):
            n = jnp.linalg.norm(x, axis=-1, keepdims=True)
            return x / jnp.maximum(n, 1e-12) * SCALE * gamma
        xn = rmsnorm(x, norm_gamma)
        sn = rmsnorm(slot_embeds, slot_norm_gamma)
        logits = jnp.einsum('bnd,esd->bnes', xn, sn)
        dispatch = jax.nn.softmax(logits, axis=1)
        b, n, e, s = logits.shape
        combine = jax.nn.softmax(logits.reshape(b, n, e * s), axis=-1)
        slots = jnp.einsum('bnd,bnes->besd', xn, dispatch)
        h = jnp.einsum('besd,edh->besh', slots, w1) + b1[None, :, None, :]
        h = jax.nn.gelu(h, approximate=False)
        eo = jnp.einsum('besh,ehd->besd', h, w2) + b2[None, :, None, :]
        eo = eo.reshape(b, e * s, DIM)
        out = jnp.einsum('bmd,bnm->bnd', eo, combine)
        return out

    def _L1_attn_ref(x, w_qkv, b_qkv, w_out, b_out):
        import jax, jax.numpy as jnp
        import numpy as np
        B, T, D, H = (2, 256, 128, 16)
        Dh = D // H

        def _rope(q, k):
            t = q.shape[2]
            dh = q.shape[3]
            inv_freq = 1.0 / 10000.0 ** (jnp.arange(0, dh, 2, dtype=jnp.float32) / dh)
            pos = jnp.arange(t, dtype=jnp.float32)
            freqs = pos[:, None] * inv_freq[None, :]
            sin = jnp.sin(freqs)[None, None]
            cos = jnp.cos(freqs)[None, None]

            def rot(x):
                xe, xo = (x[..., ::2], x[..., 1::2])
                re = xe * cos - xo * sin
                ro = xe * sin + xo * cos
                return jnp.stack([re, ro], axis=-1).reshape(x.shape)
            return (rot(q), rot(k))
        b, t, d = x.shape
        qkv = x @ w_qkv.T + b_qkv
        q, k, v = jnp.split(qkv, 3, axis=-1)
        q = q.reshape(b, t, H, Dh).transpose(0, 2, 1, 3)
        k = k.reshape(b, t, H, Dh).transpose(0, 2, 1, 3)
        v = v.reshape(b, t, H, Dh).transpose(0, 2, 1, 3)
        q, k = _rope(q, k)
        scores = jnp.einsum('bhtd,bhsd->bhts', q, k) / jnp.sqrt(jnp.float32(Dh))
        causal = jnp.tril(jnp.ones((t, t), dtype=bool))[None, None]
        scores = jnp.where(causal, scores, -jnp.inf)
        probs = jax.nn.softmax(scores, axis=-1)
        out = jnp.einsum('bhts,bhsd->bhtd', probs, v)
        out = out.transpose(0, 2, 1, 3).reshape(b, t, d)
        return out @ w_out.T + b_out

    def _L1_ffn_ref(x, wg, bg, w1, b1, w2, b2, gamma, beta):
        import jax, jax.numpy as jnp
        import numpy as np
        N_EXPERTS = 16
        TOPK = 2
        CAPACITY_FACTOR = 1.0
        EPS_GATE = 1e-06
        LN_EPS = 1e-05
        B, S, D = x.shape
        E = wg.shape[1]
        capacity = int(CAPACITY_FACTOR * B)
        scores = jax.nn.softmax(x @ wg + bg, axis=-1)
        _, top_i = jax.lax.top_k(scores, TOPK)
        mask = jax.nn.one_hot(top_i, E, dtype=scores.dtype).sum(-2)
        masked = scores * mask
        denom = masked.sum(0, keepdims=True) + EPS_GATE
        route = masked / denom * capacity
        route_e = jnp.transpose(route, (2, 0, 1))
        max_len = S // 2
        _, seq_ids = jax.lax.top_k(route_e, max_len)
        seq_ids = jnp.sort(seq_ids, axis=-1)
        b_idx = jnp.arange(B)[None, :, None]
        xg = x[b_idx, seq_ids]
        h = jnp.einsum('ebld,edf->eblf', xg, w1) + b1[:, None, None, :]
        h = jax.nn.gelu(h, approximate=False)
        out = jnp.einsum('eblf,efd->ebld', h, w2) + b2[:, None, None, :]
        outs = jnp.zeros_like(x).at[b_idx, seq_ids].add(out)
        z = x + outs
        mu = z.mean(-1, keepdims=True)
        var = ((z - mu) ** 2).mean(-1, keepdims=True)
        return (z - mu) / jnp.sqrt(var + LN_EPS) * gamma + beta
    x = L0_attn_x
    xn = _layernorm(x, axis=-1)
    s = _L0_attn_ref(xn, L0_attn_Wqkv, L0_attn_bqkv, L0_attn_Wproj, L0_attn_bproj)
    g = _silu(_L0_ffn_ref(xn, L0_ffn_norm_gamma, L0_ffn_slot_norm_gamma, L0_ffn_slot_embeds, L0_ffn_w1, L0_ffn_b1, L0_ffn_w2, L0_ffn_b2))
    x = x + s * g
    xn = _layernorm(x, axis=-1)
    s = _L1_attn_ref(xn, L1_attn_w_qkv, L1_attn_b_qkv, L1_attn_w_out, L1_attn_b_out)
    g = _silu(_L1_ffn_ref(xn, L1_ffn_wg, L1_ffn_bg, L1_ffn_w1, L1_ffn_b1, L1_ffn_w2, L1_ffn_b2, L1_ffn_gamma, L1_ffn_beta))
    x = x + s * g
    return x

_drawn_inputs = setup_inputs


def setup_inputs(seed=0):
    import zlib

    import numpy as np

    out = dict(_drawn_inputs(seed))
    spreads = {'L0_ffn_norm_gamma': (1.0, 0.6),
     'L0_ffn_slot_norm_gamma': (1.0, 0.6),
     'L0_ffn_b1': (0.0, 0.8),
     'L0_ffn_b2': (0.0, 0.8),
     'L1_attn_b_qkv': (0.0, 0.8),
     'L1_attn_b_out': (0.0, 0.8),
     'L1_ffn_bg': (0.0, 1.836),
     'L1_ffn_b1': (0.0, 2.0),
     'L1_ffn_b2': (0.0, 2.0),
     'L1_ffn_gamma': (1.0, 0.6),
     'L1_ffn_beta': (0.0, 2.0)}
    factors = {'L0_attn_Wqkv': 8.0,
     'L0_attn_bqkv': 8.0,
     'L0_attn_Wproj': 8.0,
     'L0_attn_bproj': 8.0,
     'L0_ffn_slot_embeds': 8.0,
     'L0_ffn_w1': 8.0,
     'L0_ffn_w2': 8.0,
     'L1_ffn_w1': 24.609,
     'L1_ffn_w2': 19.399,
     'L1_attn_w_qkv': 3.207,
     'L1_ffn_wg': 5.668}
    for name, (base, spread) in spreads.items():
        noise = np.random.default_rng([zlib.crc32(name.encode()), seed]).standard_normal(out[name].shape)
        drawn = base * np.exp(spread * noise) if base else spread * noise
        out[name] = jnp.asarray(drawn.astype(out[name].dtype))
    for name, factor in factors.items():
        out[name] = (out[name] * factor).astype(out[name].dtype)
    return out
```

```python
from contextlib import ExitStack

import concourse.bass as bass
import numpy as np
from concourse import mybir

F32 = mybir.dt.float32
BF16 = mybir.dt.bfloat16
I32 = mybir.dt.int32
ALU = mybir.AluOpType
ACT = mybir.ActivationFunctionType
AX = mybir.AxisListType

P = 128
B, T, E = 2, 1024, 128
NT = B * T // P
TB = T // P
H, D = 16, 8
HG = 4
GB = H // HG
NG = B * GB
SCALE = float(D) ** -0.5
TERMS = 9
KR = TERMS * D
KM = KR + 2
VC = D + 1
VP = 32
NEG = -1.0e30
BANK = 512
LN_EPS = 1e-5
ROOT = float(E) ** 0.5

NE0, SL0, HID0 = 8, 64, 512
NB0 = NE0 * SL0 // P
HC0 = HID0 // P
NE1, F1 = 16, 32
FC1 = NE1 * F1 // P
CAP = T // 2
QC = 4
QW = T // QC
BITS = 30

STEPS = [
    [(0, 0, 0)],
    [(1, 128, 0), (7, 896, 896)],
    [(2, 256, 0), (6, 768, 768)],
    [(3, 384, 0), (5, 640, 640)],
    [(4, 512, 0)],
]
WIDTH = [1024, 1024, 1024, 1024, 512]
MAX_COST = 40
FEED = 600
START = 4000
SLOT = [0, 1, 0, 1, 2]
NX = len(STEPS) * HG

MAXES = [
    ([(0, 0, 128), (4, 512, 128)], 0),
    ([(1, 0, 256), (5, 512, 256)], 1),
    ([(2, 0, 384)], 2),
    ([(6, 512, 384)], 10),
    ([(3, 0, 512)], 3),
    ([(4, 0, 512)], 4),
    ([(5, 0, 512)], 5),
    ([(6, 0, 512)], 6),
    ([(7, 0, 512)], 7),
    ([(7, 512, 512)], 11),
]
NM = len(MAXES) * HG
MT = NM + 1


def pv_rows(step):
    rows = []
    for j, q0, col in STEPS[step]:
        if q0 < BANK:
            rows.append((j, q0, BANK - q0, col))
            rows.append((j, BANK, BANK, col + BANK - q0))
        else:
            rows.append((j, q0, T - q0, col))
    return rows


def turn_order(has_prev, has_this, has_next):
    work = []
    for n in range(NX):
        s, h = divmod(n, HG)
        if has_this:
            work.append((("exp", n), WIDTH[s] + P))
        if s == 0 and h == 1 and has_prev:
            work.append((("pv", 1, len(STEPS) - 1, 0), 2 * BANK))
        if s == 0 and h == 3 and has_prev:
            work.append((("out",), 2 * BANK))
        if s >= 1 and has_this:
            rows = len(pv_rows(s - 1))
            for k, (_, _, w, _) in enumerate(pv_rows(s - 1)):
                if h == HG - min(rows, HG - 1) + k:
                    work.append((("pv", 0, s - 1, k), 4 * w))
    order, m, done, given = [], 0, 0, START if has_this else 0
    work.append((None, 0))
    for item, columns in work:
        while has_next and m < NM and (given <= done + FEED or item is None):
            width = sum(w for _, _, w in MAXES[m % len(MAXES)][0])
            order.append(("max", m))
            m, given, done = m + 1, given + width * MAX_COST // 16 + 150, done + width + P
            if m == NM:
                late = len(order)
        if item is not None:
            order.append(item)
            done += columns
    if has_next:
        order.insert(min(len(order), late + 3), ("shift",))
    return order


class Group:

    def __init__(self, g, r, nth):
        self.g, self.r, self.nth = g, r, nth

    def next(self):
        return Group(self.g + 1, 1 - self.r, self.nth + self.r)


def all_turns(eng, turn):
    turn(Group(-1, 1, 0), False, False, True)
    turn(Group(0, 0, 1), False, True, True)
    with eng.Fori(0, NG // 2 - 1) as it:
        turn(Group(it * 2 + 1, 1, it + 1), True, True, True)
        turn(Group(it * 2 + 2, 0, it + 2), True, True, True)
    turn(Group(NG - 1, 1, NG // 2), True, True, False)
    turn(Group(NG, 0, NG // 2 + 1), True, False, False)


class Chain:

    def __init__(self, eng, sem):
        self.eng, self.sem, self.n = eng, sem, 0

    def link(self, ins):
        self.n += 1
        ins.then_inc(self.sem, 1)
        self.eng.wait_ge(self.sem, self.n)


def wait(eng, sem, value):
    if not isinstance(value, int) or value > 0:
        eng.wait_ge(sem, value)


class Named:
    pass


def block_kernel(nc, a, out):
    ctx = ExitStack()
    with ctx:
        def sb(name, shape, dt=F32):
            return ctx.enter_context(nc.sbuf_tensor(name, shape, dt))

        def sem(name):
            return ctx.enter_context(nc.semaphore(name))

        q_dram = [nc.dram_tensor(f"q_thirds{n}", [3, B * E, T], BF16, kind="Internal").ap() for n in range(2)]
        k_dram = [nc.dram_tensor(f"k_thirds{n}", [3, B * E, T], BF16, kind="Internal").ap() for n in range(2)]

        x = sb("x", [P, NT, E])
        xn = sb("xn", [P, NT, E])
        xnT = sb("xnT", [P, NT * P])
        rot = sb("rot", [P, 2, T])
        ident = sb("ident", [P, P])
        identb = sb("identb", [P, P], BF16)
        maskq = sb("maskq", [P, P], BF16)
        maskk = sb("maskk", [P, P], BF16)
        gate = sb("gate", [P, NT, E])
        small = sb("small", [P, 16, 16])
        mv = sb("mv", [P, NT, 2])
        bnst = sb("bnst", [P, NT, 6])
        wqk = sb("wqk", [P, 4, E])
        wv = sb("wv", [P, E])
        wp = sb("wp", [P, E])
        bqk = sb("bqk", [P, 4])
        bvb = sb("bvb", [P, E])
        bpb = sb("bpb", [P, E])
        rope = sb("rope", [P, 2, 2, 2, BANK])
        third = sb("third", [P, 2, 2, 3, BANK], BF16)
        vals = sb("vals", [P, NG, TB, HG * VC])
        vgrp = sb("vgrp", [P, 2, TB, HG, VP])
        maxes = sb("maxes", [P, HG, 12])
        shift = sb("shift", [P, TB, 2, HG], BF16)
        rden = sb("rden", [P, TB, HG])
        R1 = sb("R1", [P, 8192])
        R2 = sb("R2", [P, 16384])
        R3 = sb("R3", [P, 4608])

        qop = R1[:, 0:4096].bitcast(BF16).rearrange("p (r h t) -> p r h t", r=2, h=HG)
        kop = R1[:, 4096:8192].bitcast(BF16).rearrange("p (r h t) -> p r h t", r=2, h=HG)
        probs = [R2[:, 0:4096].rearrange("p (h t) -> p h t", h=HG),
                 R2[:, 4096:8192].rearrange("p (h t) -> p h t", h=HG),
                 R2[:, 8192:10240].rearrange("p (h t) -> p h t", h=HG)]
        att = R2[:, 10240:12288].rearrange("p (i g c) -> p i g c", g=NG, i=TB)
        attT = R2[:, 12288:14336]
        outT = R2[:, 14336:15360]
        shiftT = R2[0:2 * HG, 15360:15872].bitcast(BF16)
        prod = R2[:, 0:2048].rearrange("p (t e) -> p t e", t=NT)

        w1s = R1[:, 0:4096].rearrange("p (e f) -> p e f", e=NE0)
        w2s = R1[:, 4096:8192].rearrange("p (e c d) -> p e c d", e=NE0, c=HC0)
        combT = R2[:, 0:8192].rearrange("p (t k c) -> p t k c", t=NT, k=NB0)
        xr = R2[:, 8192:10240].rearrange("p (t e) -> p t e", t=NT)
        xrT = R2[:, 10240:12288]
        dispT = R2[:, 12288:14336].rearrange("p (r t) -> p r t", r=2)
        disp = R2[:, 14336:16384].rearrange("p (r i c) -> p r i c", r=2, i=TB)
        comb = R3[:, 0:1024].rearrange("p (r c) -> p r c", r=2)
        slots = R3[:, 1024:2048].rearrange("p (u c) -> p u c", u=B * NB0)
        slotsT = R3[:, 2048:3072].rearrange("p (b c) -> p b c", b=B)
        hidT = R3[:, 0:1024].rearrange("p (r c n) -> p r c n", r=2, c=HC0)
        eo = disp.rearrange("p r i c -> p (r i c)")[:, 0:1024].rearrange("p (b k d) -> p b k d", b=B, k=NB0)
        semb = R3[:, 3072:3584].rearrange("p (k d) -> p k d", k=NB0)
        semT = R3[:, 3584:4096]
        b2b = R3[:, 4096:4608].rearrange("p (k d) -> p k d", k=NB0)
        gam0 = sb("gam0", [P, 2, E])
        b1c = sb("b1c", [P, NE0, HC0])
        rhid = R2[:, 0:8192].rearrange("p (f t) -> p f t", f=FC1)
        z = R2[:, 8192:10240].rearrange("p (t e) -> p t e", t=NT)
        route = R2[:, 10240:10496].rearrange("p (i b e) -> p i b e", i=TB, b=B)
        sc = [R2[:, 10496 + 256 * n:10752 + 256 * n].rearrange("p (t e) -> p t e", t=NT) for n in range(6)]
        rows = R2[:, 12288:12544]
        hit = R2[:, 12544:12800]
        greater = R2[:, 12800:13056]
        equal = R2[:, 13056:13312]
        prefix = R2[:, 13312:13568]
        nought = R2[:, 13568:13824]
        taken = R2[:, 13824:14080]
        takenb = R2[:, 14080:14208].bitcast(BF16)
        rw1 = R3[:, 0:512]
        rw2 = R3[:, 512:1024].rearrange("p (f d) -> p f d", f=FC1)
        rb2 = R2[:, 14336:15360].rearrange("p (q b d) -> p q b d", q=QC, b=B)
        gam1 = R3[:, 1280:1408]
        bet1 = R3[:, 1408:1536]
        blocksum = R3[:, 1536:1664]
        before = R3[:, 1664:1792]
        bgb = R3[:, 1792:1808]
        wg = R3[:, 1808:1824]
        rb1 = R3[:, 1824:1828]
        rank = R3[:, 1832:1848].rearrange("p (o e) -> p o e", o=1)
        spread = R3[:, 2048:4096].bitcast(BF16).rearrange("p (q b f c) -> p q b f c", q=QC, b=B, f=FC1)
        word = sb("word", [P, 4], I32)
        fbit = sb("fbit", [P, 1])
        count = sb("count", [P, 2])
        need = sb("need", [P, 1])

        ps = ctx.enter_context(nc.psum_tensor("ps", [P, 8, BANK], F32))
        flat = ps[:, :, :].rearrange("p n c -> p (n c)")

        def bank(n):
            return ps[:, n, :]

        def quarter(n, k):
            return ps[:, n, P * k:P * k + P]

        S = []
        for L in range(2):
            s = Named()
            s.weights = sem(f"weights{L}")
            s.ffn_weights = sem(f"ffn_weights{L}")
            s.variance = sem(f"variance{L}")
            s.deviation = sem(f"deviation{L}")
            s.xn = sem(f"xn{L}")
            s.xn_tr = sem(f"xn_tr{L}")
            s.xnT = sem(f"xnT{L}")
            s.v_ps = sem(f"v_ps{L}")
            s.v = sem(f"v{L}")
            s.qk_ps = sem(f"qk_ps{L}")
            s.roped = sem(f"roped{L}")
            s.summed = sem(f"summed{L}")
            s.high = sem(f"high{L}")
            s.less_high = sem(f"less_high{L}")
            s.middle = sem(f"middle{L}")
            s.low = sem(f"low{L}")
            s.stored = [sem(f"stored{L}_{r}") for r in range(2)]
            s.loaded = [[sem(f"loaded{L}_{r}_{n}") for n in range(2)] for r in range(2)]
            s.shifted = [sem(f"shifted{L}_{r}") for r in range(2)]
            s.kop_ones = sem(f"kop_ones{L}")
            s.vgrp = sem(f"vgrp{L}")
            s.max_ps = sem(f"max_ps{L}")
            s.max_read = sem(f"max_read{L}")
            s.max_own = sem(f"max_own{L}")
            s.shift = sem(f"shift{L}")
            s.shift_tr = sem(f"shift_tr{L}")
            s.shift_read = sem(f"shift_read{L}")
            s.exp_ps = sem(f"exp_ps{L}")
            s.exp = sem(f"exp{L}")
            s.pv = sem(f"pv{L}")
            s.outT = sem(f"outT{L}")
            s.out_tr = sem(f"out_tr{L}")
            s.out_own = sem(f"out_own{L}")
            s.att = sem(f"att{L}")
            s.att_tr = sem(f"att_tr{L}")
            s.attT = sem(f"attT{L}")
            s.proj = sem(f"proj{L}")
            s.gate = sem(f"gate{L}")
            s.x = sem(f"x{L}")
            S.append(s)
        s0 = Named()
        s0.xr = sem("soft_xr")
        s0.xr_tr = sem("soft_xr_tr")
        s0.xrT = sem("soft_xrT")
        s0.emb_sq = sem("soft_emb_sq")
        s0.emb_dev = sem("soft_emb_dev")
        s0.emb = sem("soft_emb")
        s0.emb_tr = sem("soft_emb_tr")
        s0.embT = sem("soft_embT")
        s0.lg_ps = sem("soft_lg_ps")
        s0.row_max = sem("soft_row_max")
        s0.comb = sem("soft_comb")
        s0.comb_tr = sem("soft_comb_tr")
        s0.combT = sem("soft_combT")
        s0.lt_ps = sem("soft_lt_ps")
        s0.col_max = sem("soft_col_max")
        s0.dispT = sem("soft_dispT")
        s0.disp_tr = sem("soft_disp_tr")
        s0.disp = sem("soft_disp")
        s0.slot_ps = sem("soft_slot_ps")
        s0.slots = sem("soft_slots")
        s0.slot_tr = sem("soft_slot_tr")
        s0.slotsT = sem("soft_slotsT")
        s0.hid_ps = sem("soft_hid_ps")
        s0.hid = sem("soft_hid")
        s0.eo_ps = sem("soft_eo_ps")
        s0.eo = sem("soft_eo")
        s0.mix_ps = sem("soft_mix_ps")
        s0.rsum = sem("soft_rsum")
        s1 = Named()
        s1.lg_ps = sem("routed_lg_ps")
        s1.logit = sem("routed_logit")
        s1.e_s = sem("routed_e_s")
        s1.route = sem("routed_route")
        s1.route_tr = sem("routed_route_tr")
        s1.count = sem("routed_count")
        s1.total = sem("routed_total")
        s1.offs = sem("routed_offs")
        s1.taken = sem("routed_taken")
        s1.hid_ps = sem("routed_hid_ps")
        s1.hid = sem("routed_hid")
        s1.rep_ps = sem("routed_rep_ps")
        s1.masked = sem("routed_masked")
        s1.out_ps = sem("routed_out_ps")
        s1.z = sem("routed_z")
        s1.var = sem("routed_var")
        s1.dev = sem("routed_dev")
        s1.pre = sem("routed_pre")
        s1.own = sem("routed_own")
        s_const = sem("constants")
        s_x = sem("x_in")
        s_vpad = sem("value_padding")
        s_dve = sem("vector_own")
        s_pool = sem("pool_own")
        s_out = sem("out_stored")

        block = ctx.enter_context(nc.Block())

        @block.sync
        def _(sp):
            sp.dma_start(x[:, :, :], a["x"].rearrange("b (i p) e -> p (b i) e", p=P)).then_inc(s_x, 16)
            for dst, name in ((ident, "ident"), (identb, "identb"), (maskq, "maskq"), (maskk, "maskk")):
                sp.dma_start(dst[:, :], a[name]).then_inc(s_const, 16)
            sp.dma_start(rot[:, :, :], a["rot"]).then_inc(s_const, 16)

            def load_block_weights(L, s):
                if L:
                    sp.wait_ge(S[0].proj, 4)
                sp.dma_start(wqk[:, :, :], a[f"wqk{L}"]).then_inc(s.weights, 16)
                sp.dma_start(wv[:, :], a[f"wv{L}"]).then_inc(s.weights, 16)
                sp.dma_start(wp[:, :], a[f"wp{L}"]).then_inc(s.weights, 16)
                sp.dma_start(bqk[:, :], a[f"bqk{L}"]).then_inc(s.weights, 16)
                sp.dma_start(bvb[:, :], a[f"bvb{L}"]).then_inc(s.weights, 16)
                if L:
                    sp.wait_ge(S[0].x, 4)
                sp.dma_start(bpb[:, :], a[f"bpb{L}"]).then_inc(s.weights, 16)

            def store_thirds(L, s):
                for c in range(4):
                    b, half = divmod(c, 2)
                    sp.wait_ge(s.low, c + 1)
                    for n, dram in enumerate((q_dram[L], k_dram[L])):
                        sp.dma_start(dram[:, b * E:b * E + E, half * BANK:half * BANK + BANK].rearrange("a e t -> e a t"),
                                     third[:, c % 2, n, :, :]).then_inc(s.stored[c % 2], 16)

            def load_operands(L, s, g, r):
                q_rows = q_dram[L][:, bass.ds(g * (HG * D), HG * D), :].rearrange("a (d h) t -> a d (h t)", h=HG)
                k_rows = k_dram[L][:, bass.ds(g * (HG * D), HG * D), :].rearrange("a (d h) t -> a d (h t)", h=HG)
                for n in range(2):
                    heads = slice(2 * n, 2 * n + 2)
                    span = slice(2 * n * T, 2 * n * T + 2 * T)
                    for i in range(3):
                        rows_i = slice(3 * D * i, 3 * D * i + 3 * D)
                        sp.dma_start(qop[rows_i, r, heads, :].rearrange("p h t -> p (h t)"),
                                     q_rows[i:i + 1, :, span].to_broadcast([3, D, 2 * T])).then_inc(s.loaded[r][n], 16)
                        sp.dma_start(kop[rows_i, r, heads, :].rearrange("p h t -> p (h t)"),
                                     k_rows[:, :, span]).then_inc(s.loaded[r][n], 16)

            load_block_weights(0, S[0])
            sp.dma_start(semb, a["slot_emb"]).then_inc(s0.emb_sq, 16)
            sp.dma_start(gam0[:, :, :], a["gam0"]).then_inc(S[0].ffn_weights, 16)
            sp.dma_start(w1s, a["w1_0"]).then_inc(S[0].ffn_weights, 16)
            sp.dma_start(w2s, a["w2_0"]).then_inc(S[0].ffn_weights, 16)
            sp.dma_start(b1c[:, :, :], a["b1_0"]).then_inc(S[0].ffn_weights, 16)
            sp.dma_start(b2b, a["b2_0"]).then_inc(S[0].ffn_weights, 16)
            for L in range(2):
                s = S[L]
                if L:
                    load_block_weights(1, s)
                    for dst, name in ((wg, "wg"), (bgb, "bgb"), (rw1, "rw1"), (rw2, "rw2"), (rb1, "rb1"), (rb2, "rb2"),
                                      (gam1, "gam1"), (bet1, "bet1"), (blocksum, "blocksum"), (before, "before"),
                                      (rank, "rank"), (spread, "spread")):
                        sp.dma_start(dst, a[name]).then_inc(s.ffn_weights, 16)
                store_thirds(L, s)
                sp.wait_ge(s.kop_ones, 2)
                for r in range(2):
                    sp.wait_ge(s.stored[r], 64)
                load_operands(L, s, 0, 0)
                load_operands(L, s, 1, 1)
                with sp.Fori(0, NG // 2 - 1) as it:
                    for r in range(2):
                        sp.wait_ge(s.exp_ps, it * (2 * NX) + NX * (r + 1))
                        load_operands(L, s, it * 2 + (2 + r), r)
            for c in range(4):
                sp.wait_ge(S[1].x, c + 1)
                b, half = divmod(c, 2)
                sp.dma_start(out[b, half * BANK:half * BANK + BANK, :].rearrange("(i p) e -> p i e", p=P),
                             x[:, 4 * c:4 * c + 4, :]).then_inc(s_out, 16)
            sp.wait_ge(s_out, 64)

        @block.gpsimd
        def _(pool):
            pool.memset(vgrp[:, 0], 0.0)
            pool.memset(vgrp[:, 1], 0.0)
            pool.memset(vals[:, :, :, :], 1.0).then_inc(s_vpad, 1)
            pool.wait_ge(s_vpad, 1)
            for L in range(2):
                s = S[L]
                for c in range(4):
                    r = c % 2
                    pool.wait_ge(s.roped, c + 1)
                    pool.tensor_tensor(rope[:, r, 0], rope[:, r, 0], rope[:, r, 1], ALU.add).then_inc(s.summed, 1)
                    pool.wait_ge(s.summed, c + 1)
                    pool.wait_ge(s.high, c + 1)
                    pool.tensor_tensor(rope[:, r, 0], rope[:, r, 0], third[:, r, :, 0, :],
                                       ALU.subtract).then_inc(s.less_high, 1)
                    pool.wait_ge(s.less_high, c + 1)
                    pool.wait_ge(s.middle, c + 1)
                    pool.tensor_tensor(third[:, r, :, 2, :], rope[:, r, 0], third[:, r, :, 1, :],
                                       ALU.subtract).then_inc(s.low, 1)
                if L == 0:
                    pool.wait_ge(s0.eo_ps, NE0)
                else:
                    pool.wait_ge(S[0].exp_ps, NG * NX)
                pool.wait_ge(s.low, 4)
                for r in range(2):
                    pool.memset(kop[64:KM, r], 1.0).then_inc(s.kop_ones, 1)
                pool.wait_ge(s.kop_ones, 2)
                pool.wait_ge(s.v, NT)
                if L:
                    pool.wait_ge(S[0].pv, NG * len(STEPS))

                def gather_values(g, r):
                    pool.tensor_copy(vgrp[:, r, :, :, 0:VC].rearrange("p j h c -> p (j h) c"),
                                     vals[:, bass.ds(g, 1), :, :].rearrange("p g j (h c) -> p (g j h) c", h=HG)
                                     ).then_inc(s.vgrp, 1)

                gather_values(0, 0)
                gather_values(1, 1)
                with pool.Fori(0, NG // 2 - 1) as it:
                    for r in range(2):
                        pool.wait_ge(s.pv, it * (2 * len(STEPS)) + len(STEPS) * (r + 1))
                        gather_values(it * 2 + (2 + r), r)

        @block.scalar
        def _(act):
            act.wait_ge(s_const, 80)

            def deviations(L, s):
                act.wait_ge(s.variance, 1)
                act.activation(small[:, 1, :], small[:, 0, :], ACT.Sqrt).then_inc(s.deviation, 1)
                if L == 0:
                    act.activation(small[:, 2, :], mv[:, :, 1], ACT.Sqrt, scale=float(E)).then_inc(s.deviation, 1)
                    act.wait_ge(s0.emb_sq, 16)
                    for k in range(NB0):
                        last = act.activation(slots[:, k, :], semb[:, k, :], ACT.Square,
                                              accum_out=small[:, 3, k:k + 1])
                    last.then_inc(s0.emb_sq, 1)
                    act.wait_ge(s0.emb_sq, 17)
                    act.activation(small[:, 4, 0:NB0], small[:, 3, 0:NB0], ACT.Sqrt).then_inc(s0.emb_dev, 1)

            def take_xnT(s):
                for c in range(4):
                    act.wait_ge(s.xn_tr, c + 1)
                    act.activation(xnT[:, BANK * c:BANK * c + BANK], bank(c), ACT.Copy).then_inc(s.xnT, 1)

            def split(s):
                for c in range(4):
                    r = c % 2
                    act.wait_ge(s.summed, c + 1)
                    if c >= 2:
                        act.wait_ge(s.stored[r], 32)
                    act.activation(third[:, r, :, 0, :], rope[:, r, 0], ACT.Copy).then_inc(s.high, 1)
                    act.wait_ge(s.less_high, c + 1)
                    act.activation(third[:, r, :, 1, :], rope[:, r, 0], ACT.Copy).then_inc(s.middle, 1)

            def soft_experts():
                for c in range(4):
                    act.wait_ge(s0.xr_tr, c + 1)
                    act.activation(xrT[:, BANK * c:BANK * c + BANK], bank(c), ACT.Copy).then_inc(s0.xrT, 1)
                act.wait_ge(s0.emb_tr, 1)
                act.activation(semT, bank(4), ACT.Copy).then_inc(s0.embT, 1)
                for t in range(NT):
                    act.wait_ge(s0.row_max, t + 1)
                    if t >= 2:
                        act.wait_ge(s0.comb_tr, t - 1)
                    act.activation(comb[:, t % 2, :], bank(t % 2), ACT.Exp, bias=small[:, 5, t:t + 1],
                                   accum_out=small[:, 6, t:t + 1]).then_inc(s0.comb, 1)
                for u in range(B * NB0):
                    act.wait_ge(s0.col_max, u + 1)
                    if u >= 2:
                        act.wait_ge(s0.disp_tr, u - 1)
                    act.activation(dispT[:, u % 2, :], flat[:, 1024 * (2 + u % 2):1024 * (3 + u % 2)], ACT.Exp,
                                   bias=small[:, 7, u:u + 1], accum_out=small[:, 8, u:u + 1]).then_inc(s0.dispT, 1)
                    act.wait_ge(s0.disp_tr, u + 1)
                    if u >= 2:
                        act.wait_ge(s0.slot_ps, u - 1)
                    act.activation(disp[:, u % 2].rearrange("p i c -> p (i c)"),
                                   flat[:, 1024 * (u % 2):1024 * (u % 2) + 1024], ACT.Copy).then_inc(s0.disp, 1)
                    act.wait_ge(s0.slot_tr, u + 1)
                    b, k = divmod(u, NB0)
                    act.activation(slotsT[:, b, P * k:P * k + P], quarter(5 + 2 * (u % 2), 0), ACT.Copy
                                   ).then_inc(s0.slotsT, 1)
                act.wait_ge(S[0].ffn_weights, 80)
                for e in range(NE0):
                    act.wait_ge(s0.hid_ps, e + 1)
                    if e >= 2:
                        act.wait_ge(s0.eo_ps, e - 1)
                    for c in range(HC0):
                        last = act.activation(hidT[:, e % 2, c, :], quarter(e % 2, c), ACT.Gelu,
                                              bias=b1c[:, e, c:c + 1])
                    last.then_inc(s0.hid, 1)
                act.wait_ge(s0.rsum, 1)
                for t in range(NT):
                    act.wait_ge(s0.mix_ps, t // 4 + 1)
                    act.activation(gate[:, t, :], quarter((t // 4) % 4, t % 4), ACT.Silu,
                                   scale=small[:, 9, t:t + 1]).then_inc(S[0].gate, 1)

            def routed_experts():
                act.wait_ge(s1.logit, 1)
                act.activation(sc[1], sc[0], ACT.Exp).then_inc(s1.e_s, 1)
                for c in range(4):
                    for f in range(FC1):
                        n = c * FC1 + f
                        act.wait_ge(s1.hid_ps, n + 1)
                        act.activation(rhid[:, f, BANK * c:BANK * c + BANK], bank(4 + n % 4), ACT.Gelu,
                                       bias=rb1[:, f:f + 1]).then_inc(s1.hid, 1)
                act.wait_ge(s1.var, 1)
                act.activation(small[:, 1, :], small[:, 0, :], ACT.Sqrt).then_inc(s1.dev, 1)
                for c in range(4):
                    act.wait_ge(s1.pre, c + 1)
                    act.activation(gate[:, 4 * c:4 * c + 4, :], z[:, 4 * c:4 * c + 4, :], ACT.Silu
                                   ).then_inc(S[1].gate, 4)

            def attention(L, s):
                def turn(now, has_prev, has_this, has_next):
                    for what, *arg in turn_order(has_prev, has_this, has_next):
                        if what == "exp":
                            n = arg[0]
                            step, h = divmod(n, HG)
                            w = WIDTH[step]
                            act.wait_ge(s.exp_ps, now.g * NX + (n + 1))
                            wait(act, s.pv, now.g * len(STEPS) + [-2, -1, 1, 2, 0][step])
                            act.activation(probs[SLOT[step]][:, h, 0:w],
                                           flat[:, 1024 * (n % 2):1024 * (n % 2) + w],
                                           ACT.Exp, scale=SCALE).then_inc(s.exp, 1)
                        elif what == "out":
                            act.wait_ge(s.pv, now.g * len(STEPS))
                            act.activation(outT, flat[:, 6 * BANK:8 * BANK], ACT.Copy).then_inc(s.outT, 1)
                        elif what == "shift":
                            new = now.next()
                            act.wait_ge(s.shift_tr, new.g + 1)
                            act.activation(shiftT, bank(4 + new.r)[0:2 * HG, :].bitcast(BF16), ACT.Copy
                                           ).then_inc(s.shift_read, 1)
                            act.wait_ge(s.shift_read, new.g + 1)
                            for part in range(2):
                                act.dma_start(qop[KR + part:KR + part + 1, new.r, :, :],
                                              shiftT[HG * part:HG * part + HG, :]).then_inc(s.shifted[new.r], 16)

                all_turns(act, turn)
                for c in range(4):
                    act.wait_ge(s.att_tr, c + 1)
                    act.activation(attT[:, BANK * c:BANK * c + BANK], bank(c), ACT.Copy).then_inc(s.attT, 1)

            for L in range(2):
                deviations(L, S[L])
                take_xnT(S[L])
                split(S[L])
                if L == 0:
                    soft_experts()
                else:
                    routed_experts()
                attention(L, S[L])

        @block.vector
        def _(dve):
            own = Chain(dve, s_dve)

            def normalise(src, var_sem, dev_sem, dst, done):
                for t in range(NT):
                    last = dve.bn_stats(bnst[:, t, :], src[:, t, :])
                own.link(last)
                for t in range(NT):
                    last = dve.bn_aggr(mv[:, t, :], bnst[:, t, :])
                own.link(last)
                dve.tensor_scalar(small[:, 0, :], mv[:, :, 1], LN_EPS, None, ALU.add).then_inc(var_sem, 1)
                dve.wait_ge(dev_sem, 1)
                root, inv, step = small[:, 1, :], small[:, 10, :], small[:, 11, :]
                own.link(dve.reciprocal(inv, root))
                own.link(dve.tensor_tensor(step, inv, inv, ALU.mult))
                own.link(dve.tensor_tensor(step, step, small[:, 0, :], ALU.mult))
                own.link(dve.tensor_scalar(step, step, -0.5, 1.5, ALU.mult, ALU.add))
                own.link(dve.tensor_tensor(inv, inv, step, ALU.mult))
                for t in range(NT):
                    last = dve.tensor_scalar(dst[:, t, :], src[:, t, :], mv[:, t, 0:1], small[:, 10, t:t + 1],
                                             ALU.subtract, ALU.mult)
                    if done is not None:
                        last.then_inc(done, 1)
                return last

            def rotate(L, s):
                dve.wait_ge(s.weights, 96)
                dve.wait_ge(s_vpad, 1)
                for t in range(NT):
                    b, i = divmod(t, TB)
                    dve.wait_ge(s.v_ps, t // 4 + 1)
                    dst = vals[:, b * GB:b * GB + GB, i, :].rearrange("p g (h c) -> p g h c", c=VC)
                    dve.tensor_tensor(dst[:, :, :, 0:D],
                                      quarter(4 + t // 4, t % 4).rearrange("p (g h c) -> p g h c", g=GB, c=D),
                                      bvb[:, :].rearrange("p (g h c) -> p g h c", g=GB, c=D), ALU.add).then_inc(s.v, 1)
                dve.wait_ge(s_const, 80)
                for c in range(4):
                    r, half = c % 2, c % 2
                    if c >= 2:
                        dve.wait_ge(s.low, c - 1)
                    dve.wait_ge(s.qk_ps, c + 1)
                    for n in range(2):
                        for k in range(2):
                            last = dve.scalar_tensor_tensor(
                                rope[:, r, k, n, :], bank(4 * (1 - c % 2) + 2 * n + k), bqk[:, 2 * n + k:2 * n + k + 1],
                                rot[:, k, BANK * half:BANK * half + BANK], ALU.add, ALU.mult)
                    last.then_inc(s.roped, 1)

            def root_mean_square():
                dve.wait_ge(S[0].deviation, 2)
                norm = small[:, 12, :]
                own.link(dve.tensor_tensor(norm, small[:, 2, :], small[:, 10, :], ALU.mult))
                own.link(dve.tensor_scalar(norm, norm, 1e-12, None, ALU.max))
                own.link(dve.reciprocal(norm, norm))
                own.link(dve.tensor_scalar(norm, norm, ROOT, None, ALU.mult))
                dve.wait_ge(S[0].ffn_weights, 80)
                for t in range(NT):
                    dve.scalar_tensor_tensor(xr[:, t, :], xn[:, t, :], small[:, 12, t:t + 1], gam0[:, 0, :],
                                             ALU.mult, ALU.mult).then_inc(s0.xr, 1)
                dve.wait_ge(s0.emb_dev, 1)
                emb = small[:, 13, 0:NB0]
                own.link(dve.tensor_scalar(emb, small[:, 4, 0:NB0], 1e-12, None, ALU.max))
                own.link(dve.reciprocal(emb, emb))
                own.link(dve.tensor_scalar(emb, emb, ROOT, None, ALU.mult))
                for k in range(NB0):
                    last = dve.scalar_tensor_tensor(semb[:, k, :], semb[:, k, :], small[:, 13, k:k + 1], gam0[:, 1, :],
                                                    ALU.mult, ALU.mult)
                last.then_inc(s0.emb, 1)

            def soft_experts():
                def take_comb(t):
                    dve.wait_ge(s0.comb_tr, t + 1)
                    dve.tensor_copy(combT[:, t].rearrange("p k c -> p (k c)"), bank(2 + t % 2)).then_inc(s0.combT, 1)

                for t in range(NT):
                    dve.wait_ge(s0.lg_ps, t + 1)
                    dve.tensor_reduce(small[:, 5, t:t + 1], bank(t % 2), AX.X, ALU.max, negate=True
                                      ).then_inc(s0.row_max, 1)
                    if t:
                        take_comb(t - 1)
                take_comb(NT - 1)

                def scale_slots(u):
                    dve.wait_ge(s0.dispT, u + 1)
                    own.link(dve.reciprocal(small[:, 14, u:u + 1], small[:, 8, u:u + 1]))
                    dve.wait_ge(s0.slot_ps, u + 1)
                    dve.tensor_scalar(slots[:, u, :], quarter(4 + 2 * (u % 2), 0), small[:, 14, u:u + 1], None,
                                      ALU.mult).then_inc(s0.slots, 1)

                for u in range(B * NB0):
                    dve.wait_ge(s0.lt_ps, u + 1)
                    dve.tensor_reduce(small[:, 7, u:u + 1], flat[:, 1024 * (2 + u % 2):1024 * (3 + u % 2)], AX.X,
                                      ALU.max, negate=True).then_inc(s0.col_max, 1)
                    if u:
                        scale_slots(u - 1)
                scale_slots(B * NB0 - 1)
                dve.wait_ge(s0.comb, NT)
                dve.reciprocal(small[:, 9, :], small[:, 6, :]).then_inc(s0.rsum, 1)
                for k in range(NB0):
                    dve.wait_ge(s0.eo_ps, 2 * k + 2)
                    dve.tensor_tensor(eo[:, :, k, :], bank(4 + k % 2)[:, 0:B * E].rearrange("p (b d) -> p b d", b=B),
                                      b2b[:, k, :].unsqueeze(1).to_broadcast([P, B, E]), ALU.add).then_inc(s0.eo, 1)

            def routes():
                logit, soft, low, pick1, pick2, tmp = sc
                wide = [P, NT, NE1]
                row = small[:, 5, :]
                spread_row = row.unsqueeze(2).to_broadcast(wide)
                ranks = rank.to_broadcast(wide)
                dve.wait_ge(S[1].ffn_weights, 16 * 12)
                dve.wait_ge(s1.lg_ps, 1)
                own.link(dve.tensor_tensor(logit, bank(0)[:, 0:NT * NE1].rearrange("p (t e) -> p t e", t=NT),
                                           bgb.unsqueeze(1).to_broadcast(wide), ALU.add))
                own.link(dve.tensor_reduce(row, logit, AX.X, ALU.max))
                dve.tensor_tensor(logit, logit, spread_row, ALU.subtract).then_inc(s1.logit, 1)
                dve.wait_ge(s1.e_s, 1)
                own.link(dve.tensor_reduce(row, soft, AX.X, ALU.add))
                own.link(dve.reciprocal(row, row))
                own.link(dve.tensor_tensor(soft, soft, spread_row, ALU.mult))
                left = soft
                for pick in (pick1, pick2):
                    own.link(dve.tensor_reduce(row, left, AX.X, ALU.max))
                    own.link(dve.tensor_tensor(tmp, left, spread_row, ALU.is_equal))
                    own.link(dve.tensor_tensor(tmp, tmp, ranks, ALU.mult))
                    own.link(dve.tensor_reduce(row, tmp, AX.X, ALU.max))
                    own.link(dve.tensor_tensor(pick, tmp, spread_row, ALU.is_equal))
                    if pick is pick1:
                        own.link(dve.scalar_tensor_tensor(low, pick1, -4.0, soft, ALU.mult, ALU.add))
                        left = low
                own.link(dve.tensor_tensor(pick1, pick1, pick2, ALU.add))
                own.link(dve.tensor_tensor(pick1, pick1, soft, ALU.mult))
                masked = pick1.rearrange("p (b i) e -> p b i e", b=B)
                both = tmp[:, 0:TB, :]
                own.link(dve.tensor_tensor(both, masked[:, 0], masked[:, 1], ALU.add))
                own.link(dve.tensor_scalar(both, both, 1e-6, None, ALU.add))
                own.link(dve.reciprocal(both, both))
                own.link(dve.tensor_scalar(both, both, float(B), None, ALU.mult))
                for b in range(B):
                    last = dve.tensor_tensor(route[:, :, b, :], masked[:, b], both, ALU.mult)
                last.then_inc(s1.route, 1)
                dve.wait_ge(s1.route_tr, 1)
                for c in range(QC):
                    last = dve.tensor_copy(rows[32 * c:32 * c + 32, :], flat[0:32, BANK + QW * c:BANK + QW * c + QW])
                own.link(last)

            def search():
                thr, cand, bit, kept = (word[:, n:n + 1] for n in range(4))
                dve.memset(thr, 0)
                dve.memset(bit, 1 << (BITS - 1))
                own.link(dve.memset(fbit[:, :], float(1 << (BITS - 1))))
                with dve.Fori(0, BITS) as it:
                    base = it * 5
                    dve.tensor_tensor(cand, thr, bit, ALU.bitwise_or).then_inc(s1.own, 1)
                    dve.wait_ge(s1.own, base + 1)
                    dve.tensor_scalar(hit, rows, cand.bitcast(F32), None, ALU.is_ge, ALU.add,
                                      accum_out=count[:, 0:1]).then_inc(s1.count, 1)
                    dve.wait_ge(s1.total, it + 1)
                    dve.tensor_scalar(kept, bank(3)[:, 0:1], float(CAP), fbit[:, :], ALU.is_ge, ALU.mult
                                      ).then_inc(s1.own, 1)
                    dve.wait_ge(s1.own, base + 2)
                    dve.tensor_tensor(thr, thr, kept, ALU.bitwise_or).then_inc(s1.own, 1)
                    dve.tensor_scalar(bit, bit, 1, None, ALU.logical_shift_right).then_inc(s1.own, 1)
                    dve.tensor_scalar(fbit[:, :], fbit[:, :], 0.5, None, ALU.mult).then_inc(s1.own, 1)
                    dve.wait_ge(s1.own, base + 5)
                limit = thr.bitcast(F32)
                dve.tensor_scalar(greater, rows, limit, None, ALU.is_gt, ALU.add, accum_out=count[:, 0:1])
                dve.memset(nought, 0.0)
                own.link(dve.tensor_scalar(equal, rows, limit, None, ALU.is_equal, ALU.add, accum_out=count[:, 1:2]))
                dve.tensor_tensor_scan(prefix, equal, nought, 0.0, ALU.add, ALU.add).then_inc(s1.count, 1)
                dve.wait_ge(s1.count, BITS + 1)
                dve.wait_ge(s1.offs, 1)
                own.link(dve.tensor_scalar(need[:, :], bank(3)[:, 1:2], -1.0, float(CAP), ALU.mult, ALU.add))
                own.link(dve.scalar_tensor_tensor(equal, prefix, need[:, :], equal, ALU.is_le, ALU.mult))
                own.link(dve.tensor_tensor(taken, greater, equal, ALU.add))
                dve.tensor_copy(takenb, taken).then_inc(s1.taken, 1)

            def routed_experts():
                for c in range(4):
                    for f in range(FC1):
                        n = c * FC1 + f
                        dve.wait_ge(s1.rep_ps, n + 1)
                        dve.wait_ge(s1.hid, n + 1)
                        span = rhid[:, f, BANK * c:BANK * c + BANK]
                        dve.tensor_tensor(span, span, bank(n % 2), ALU.mult).then_inc(s1.masked, 1)
                for c in range(4):
                    dve.wait_ge(s1.out_ps, c + 1)
                    last = dve.tensor_tensor(z[:, 4 * c:4 * c + 4, :].rearrange("p t e -> p (t e)"),
                                             xn[:, 4 * c:4 * c + 4, :].rearrange("p t e -> p (t e)"),
                                             bank(4 + c), ALU.add)
                    last.then_inc(s1.z, 1)
                dve.wait_ge(s1.z, 4)
                own.link(normalise(z, s1.var, s1.dev, z, None))
                for c in range(4):
                    four = z[:, 4 * c:4 * c + 4, :]
                    last = dve.tensor_tensor(four, four, gam1.unsqueeze(1).to_broadcast([P, 4, E]), ALU.mult)
                own.link(last)
                for c in range(4):
                    four = z[:, 4 * c:4 * c + 4, :]
                    dve.tensor_tensor(four, four, bet1.unsqueeze(1).to_broadcast([P, 4, E]), ALU.add
                                      ).then_inc(s1.pre, 1)

            def attention(L, s):
                def turn(now, has_prev, has_this, has_next):
                    new = now.next()
                    for what, *arg in turn_order(has_prev, has_this, has_next):
                        if what == "max":
                            h, m = divmod(arg[0], len(MAXES))
                            segments, col = MAXES[m]
                            n, w = len(segments), segments[0][2]
                            dve.wait_ge(s.max_ps, new.g * NM + (arg[0] + 1))
                            src = bank(4 + (new.r + arg[0]) % 2)[:, 0:n * w].rearrange("p (n w) -> p n w", n=n)
                            dst = maxes[:, h, col:col + 8 * (n - 1) + 1:8] if n > 1 else maxes[:, h, col:col + 1]
                            dve.tensor_reduce(dst, src, AX.X, ALU.max).then_inc(s.max_read, 1)
                            if arg[0] == NM - 1:
                                dve.wait_ge(s.max_read, new.g * NM + NM)
                                late = maxes[:, :, 4:8]
                                dve.tensor_tensor(late, late, maxes[:, :, 8:12], ALU.max).then_inc(s.max_own, 1)
                                dve.wait_ge(s.max_own, new.g * 2 + 1)
                                top = maxes[:, :, 0:TB].rearrange("p h i -> p i h")
                                dve.tensor_scalar(shift[:, :, 0, :], top, -1.0, None, ALU.mult).then_inc(s.max_own, 1)
                                dve.wait_ge(s.max_own, new.g * 2 + 2)
                                dve.scalar_tensor_tensor(shift[:, :, 1, :], top, -1.0, shift[:, :, 0, :],
                                                         ALU.mult, ALU.subtract).then_inc(s.shift, 1)
                        elif what == "out":
                            dve.wait_ge(s.out_tr, now.g)
                            tr = flat[:, 6 * BANK:8 * BANK].rearrange("p (i h c) -> p i h c", i=TB, h=HG)
                            dve.reciprocal(rden[:, :, :], tr[:, :, :, D]).then_inc(s.out_own, 1)
                            dve.wait_ge(s.out_own, now.g)
                            dst = att[:, :, bass.ds(now.g - 1, 1), :].rearrange("p i g (h c) -> p (i g) h c", h=HG)
                            dve.tensor_tensor(dst, tr[:, :, :, 0:D],
                                              rden[:, :, :].unsqueeze(3).to_broadcast([P, TB, HG, D]), ALU.mult
                                              ).then_inc(s.att, 1)

                all_turns(dve, turn)

            def add_gated(L, s):
                dve.wait_ge(s.gate, NT)
                for c in range(4):
                    dve.wait_ge(s.proj, c + 1)
                    four = slice(4 * c, 4 * c + 4)
                    own.link(dve.tensor_tensor(prod[:, four, :], bank(4 + c).rearrange("p (t e) -> p t e", t=4),
                                               bpb[:, :].unsqueeze(1).to_broadcast([P, 4, E]), ALU.add))
                    own.link(dve.tensor_tensor(prod[:, four, :], prod[:, four, :], gate[:, four, :], ALU.mult))
                    dve.tensor_tensor(x[:, four, :], x[:, four, :], prod[:, four, :], ALU.add).then_inc(s.x, 1)
                dve.wait_ge(s.x, 4)

            dve.wait_ge(s_x, 16)
            for L in range(2):
                s = S[L]
                normalise(x, s.variance, s.deviation, xn, s.xn)
                rotate(L, s)
                if L == 0:
                    dve.wait_ge(s.xn, NT)
                    root_mean_square()
                    soft_experts()
                else:
                    routes()
                    search()
                    routed_experts()
                attention(L, s)
                add_gated(L, s)

        @block.tensor
        def _(pe):
            def mm(out_, lhsT, rhs, first=True, last=True):
                return pe.matmul(out_, lhsT, rhs, start=first, stop=last)

            def tokens_T(s):
                for c in range(4):
                    pe.wait_ge(s.xn, 4 * c + 4)
                    for k in range(4):
                        last = pe.transpose(quarter(c, k), xn[:, 4 * c + k, :], ident[:, :])
                    last.then_inc(s.xn_tr, 1)

            def project(L, s):
                pe.wait_ge(s.weights, 96)
                for c in range(4):
                    pe.wait_ge(s.xnT, c + 1)
                    for k in range(4):
                        t = 4 * c + k
                        last = mm(quarter(4 + c, k), xnT[:, P * t:P * t + P], wv[:, :])
                    last.then_inc(s.v_ps, 1)
                for c in range(4):
                    if c == 0:
                        pe.wait_ge(s.v, NT)
                    elif c >= 2:
                        pe.wait_ge(s.roped, c - 1)
                    for k in range(4):
                        last = mm(bank(4 * (1 - c % 2) + k), wqk[:, k, :], xnT[:, BANK * c:BANK * c + BANK])
                    last.then_inc(s.qk_ps, 1)

            def soft_experts():
                pe.wait_ge(S[0].roped, 4)
                for c in range(4):
                    pe.wait_ge(s0.xr, 4 * c + 4)
                    for k in range(4):
                        last = pe.transpose(quarter(c, k), xr[:, 4 * c + k, :], ident[:, :])
                    last.then_inc(s0.xr_tr, 1)
                pe.wait_ge(s0.emb, 1)
                for k in range(NB0):
                    last = pe.transpose(quarter(4, k), semb[:, k, :], ident[:, :])
                last.then_inc(s0.emb_tr, 1)
                pe.wait_ge(s0.xrT, 4)
                pe.wait_ge(s0.embT, 1)

                def comb_T(t):
                    pe.wait_ge(s0.comb, t + 1)
                    if t >= 2:
                        pe.wait_ge(s0.combT, t - 1)
                    for k in range(NB0):
                        last = pe.transpose(quarter(2 + t % 2, k), comb[:, t % 2, P * k:P * k + P], ident[:, :])
                    last.then_inc(s0.comb_tr, 1)

                for t in range(NT):
                    if t >= 2:
                        pe.wait_ge(s0.comb, t - 1)
                    mm(bank(t % 2), xrT[:, P * t:P * t + P], semT).then_inc(s0.lg_ps, 1)
                    if t:
                        comb_T(t - 1)
                comb_T(NT - 1)

                def dispatch(u):
                    b, k = divmod(u, NB0)
                    pe.wait_ge(s0.dispT, u + 1)
                    if u >= 2:
                        pe.wait_ge(s0.disp, u - 1)
                    for i in range(TB):
                        last = pe.transpose(quarter(2 * (u % 2) + i // 4, i % 4), dispT[:, u % 2, P * i:P * i + P],
                                            ident[:, :])
                    last.then_inc(s0.disp_tr, 1)
                    pe.wait_ge(s0.disp, u + 1)
                    for i in range(TB):
                        last = mm(quarter(4 + 2 * (u % 2), 0), disp[:, u % 2, i, :], xr[:, b * TB + i, :],
                                  i == 0, i == TB - 1)
                    last.then_inc(s0.slot_ps, 1)
                    pe.wait_ge(s0.slots, u + 1)
                    pe.transpose(quarter(5 + 2 * (u % 2), 0), slots[:, u, :], ident[:, :]).then_inc(s0.slot_tr, 1)

                pe.wait_ge(s0.comb, NT)
                pe.wait_ge(s0.combT, NT)
                for u in range(B * NB0):
                    b, k = divmod(u, NB0)
                    if u >= 2:
                        pe.wait_ge(s0.slotsT, u - 1)
                    for c in range(2):
                        last = mm(bank(4 + 2 * (u % 2) + c), semT[:, P * k:P * k + P],
                                  xrT[:, T * b + BANK * c:T * b + BANK * c + BANK])
                    last.then_inc(s0.lt_ps, 1)
                    if u:
                        dispatch(u - 1)
                dispatch(B * NB0 - 1)

                def expert_out(e):
                    k, low = e // 2, SL0 * (e % 2)
                    pe.wait_ge(s0.hid, e + 1)
                    if k >= 2 and e % 2 == 0:
                        pe.wait_ge(s0.eo, k - 1)
                    for b in range(B):
                        for c in range(HC0):
                            last = mm(ps[low:low + SL0, 4 + k % 2, E * b:E * b + E],
                                      hidT[:, e % 2, c, SL0 * b:SL0 * b + SL0], w2s[:, e, c, :], c == 0, c == HC0 - 1)
                    last.then_inc(s0.eo_ps, 1)

                pe.wait_ge(s0.slotsT, B * NB0)
                pe.wait_ge(S[0].ffn_weights, 80)
                for e in range(NE0):
                    if e >= 2:
                        pe.wait_ge(s0.hid, e - 1)
                    for c in range(HC0):
                        last = mm(quarter(e % 2, c), w1s[:, e, P * c:P * c + P], slotsT[:, :, SL0 * e:SL0 * e + SL0])
                    last.then_inc(s0.hid_ps, 1)
                    if e:
                        expert_out(e - 1)
                expert_out(NE0 - 1)
                pe.wait_ge(s0.eo, NB0)
                for t in range(NT):
                    for k in range(NB0):
                        last = mm(quarter(t // 4, t % 4), combT[:, t, k, :], eo[:, t // TB, k, :], k == 0, k == NB0 - 1)
                    if t % 4 == 3:
                        last.then_inc(s0.mix_ps, 1)
                pe.wait_ge(S[0].gate, NT)

            def routed_experts():
                pe.wait_ge(S[1].roped, 4)
                pe.wait_ge(S[1].ffn_weights, 16 * 12)
                for t in range(NT):
                    last = mm(bank(0)[:, NE1 * t:NE1 * t + NE1], xnT[:, P * t:P * t + P], wg)
                last.then_inc(s1.lg_ps, 1)

                def hidden(n):
                    c, f = divmod(n, FC1)
                    if n >= 4:
                        pe.wait_ge(s1.hid, n - 3)
                    mm(bank(4 + n % 4), rw1[:, P * f:P * f + P], xnT[:, BANK * c:BANK * c + BANK]
                       ).then_inc(s1.hid_ps, 1)

                for n in range(4 * FC1):
                    hidden(n)
                pe.wait_ge(s1.route, 1)
                for i in range(TB):
                    last = pe.transpose(flat[0:B * NE1, BANK + P * i:BANK + P * i + P],
                                        route[:, i].rearrange("p b e -> p (b e)"), ident[:, :])
                last.then_inc(s1.route_tr, 1)
                with pe.Fori(0, BITS) as it:
                    pe.wait_ge(s1.count, it + 1)
                    mm(bank(3)[:, 0:1], blocksum, count[:, 0:1]).then_inc(s1.total, 1)
                pe.wait_ge(s1.count, BITS + 1)
                mm(bank(3)[:, 1:2], blocksum, count[:, 0:1], True, False)
                mm(bank(3)[:, 1:2], before, count[:, 1:2], False, True).then_inc(s1.offs, 1)
                pe.wait_ge(s1.taken, 1)
                for c in range(4):
                    b = c // 2
                    for f in range(FC1):
                        n = c * FC1 + f
                        if n >= 2:
                            pe.wait_ge(s1.masked, n - 1)
                        for j in range(2):
                            q = 2 * (c % 2) + j
                            last = mm(bank(n % 2)[:, QW * j:QW * j + QW], spread[:, q, b, f, :], takenb)
                        last.then_inc(s1.rep_ps, 1)
                pe.wait_ge(s1.hid, 4 * FC1)
                for c in range(4):
                    pe.wait_ge(s1.masked, 4 * (c + 1))
                    for k in range(4):
                        t = 4 * c + k
                        b, i = divmod(t, TB)
                        for f in range(FC1):
                            mm(quarter(4 + c, k), rhid[:, f, P * t:P * t + P], rw2[:, f, :], f == 0, False)
                        q, half = divmod(i, 2)
                        last = mm(quarter(4 + c, k), taken[:, P * half:P * half + P], rb2[:, q, b, :], False, True)
                    last.then_inc(s1.out_ps, 1)
                pe.wait_ge(s1.z, 4)

            def attention(L, s):
                def turn(now, has_prev, has_this, has_next):
                    new = now.next()
                    for what, *arg in turn_order(has_prev, has_this, has_next):
                        if what == "exp":
                            n = arg[0]
                            step, h = divmod(n, HG)
                            if n == 0:
                                pe.wait_ge(s.shifted[now.r], now.nth * 32)
                            wait(pe, s.exp, now.g * NX + (n - 1))
                            for j, q0, col in STEPS[step]:
                                c = col
                                while c < col + T - q0:
                                    w = min(BANK - c % BANK, col + T - q0 - c)
                                    q = q0 + c - col
                                    diag = c == col
                                    last = mm(flat[:, 1024 * (n % 2) + c:1024 * (n % 2) + c + w],
                                              kop[0:KM, now.r, h, P * j:P * j + P], qop[0:KM, now.r, h, q:q + w],
                                              True, not diag)
                                    if diag:
                                        last = mm(flat[:, 1024 * (n % 2) + c:1024 * (n % 2) + c + P],
                                                  identb[:, :], maskk[:, :], False, True)
                                    c += w
                            last.then_inc(s.exp_ps, 1)
                        elif what == "max":
                            h, m = divmod(arg[0], len(MAXES))
                            if arg[0] % (NM // 2) == 0:
                                pe.wait_ge(s.loaded[new.r][arg[0] // (NM // 2)], new.nth * 96)
                            if arg[0] == 0:
                                wait(pe, s.max_read, new.g * NM)
                            elif arg[0] == 1:
                                wait(pe, s.shift_read, new.g)
                            else:
                                pe.wait_ge(s.max_read, new.g * NM + (arg[0] - 1))
                            dst = bank(4 + (new.r + arg[0]) % 2)
                            c = 0
                            for i, k0, w in MAXES[m][0]:
                                diag = k0 + w == P * (i + 1)
                                last = mm(dst[:, c:c + w], qop[0:KR, new.r, h, P * i:P * i + P],
                                          kop[0:KR, new.r, h, k0:k0 + w], True, not diag)
                                if diag:
                                    last = mm(dst[:, c + w - P:c + w], identb[:, :], maskq[:, :], False, True)
                                c += w
                            last.then_inc(s.max_ps, 1)
                        elif what == "shift":
                            pe.wait_ge(s.shift, new.g + 1)
                            dst = bank(4 + new.r)[0:2 * HG, :].bitcast(BF16)
                            for i in range(TB):
                                last = pe.transpose(dst[:, P * i:P * i + P],
                                                    shift[:, i].rearrange("p a h -> p (a h)"), identb[:, :])
                            last.then_inc(s.shift_tr, 1)
                        elif what == "pv":
                            back, step, row = arg
                            g, r, nth = now.g - back, (now.r + back) % 2, now.nth
                            if step == 0 and row == 0:
                                pe.wait_ge(s.vgrp, g + 1)
                                wait(pe, s.att, g)
                            if row == 0:
                                pe.wait_ge(s.exp, g * NX + HG * (step + 1))
                            j, q, w, col = pv_rows(step)[row]
                            half = q // BANK
                            done = j == (3 if half == 0 else 4)
                            for h in range(HG):
                                last = mm(ps[VP * h:VP * h + VP, 6 + half, q % BANK:q % BANK + w],
                                          vgrp[:, r, j, h, :], probs[SLOT[step]][:, h, col:col + w],
                                          j == 0, done)
                            if row == len(pv_rows(step)) - 1:
                                last.then_inc(s.pv, 1)
                        elif what == "out":
                            pe.wait_ge(s.outT, now.g)
                            for i in range(TB):
                                last = pe.transpose(quarter(6 + i // 4, i % 4), outT[:, P * i:P * i + P], ident[:, :])
                            last.then_inc(s.out_tr, 1)

                all_turns(pe, turn)
                pe.wait_ge(s.att, NG)
                for c in range(4):
                    for k in range(4):
                        b, i = divmod(4 * c + k, TB)
                        last = pe.transpose(quarter(c, k), att[:, i, GB * b:GB * b + GB, :].rearrange("p g c -> p (g c)"), ident[:, :])
                    last.then_inc(s.att_tr, 1)
                for c in range(4):
                    pe.wait_ge(s.attT, c + 1)
                    for k in range(4):
                        t = 4 * c + k
                        last = mm(quarter(4 + c, k), attT[:, P * t:P * t + P], wp[:, :])
                    last.then_inc(s.proj, 1)

            pe.wait_ge(s_const, 80)
            for L in range(2):
                s = S[L]
                tokens_T(s)
                project(L, s)
                if L == 0:
                    soft_experts()
                else:
                    routed_experts()
                attention(L, s)


def constants():
    half_type = mybir.dt.np(BF16)
    c = {}
    c["ident"] = np.eye(P, dtype=np.float32)
    c["identb"] = c["ident"].astype(half_type)
    later = np.arange(P)[None, :] > np.arange(P)[:, None]
    c["maskq"] = np.where(later, NEG, 0.0).astype(half_type)
    c["maskk"] = np.where(later.T, NEG, 0.0).astype(half_type)
    freq = (1.0 / 10000.0 ** (np.arange(0, D, 2, dtype=np.float32) / D)).astype(np.float32)
    angle = np.arange(T, dtype=np.float32)[:, None] * freq[None, :]
    feature = (np.arange(E) % (HG * D)) // HG
    cos = np.cos(angle).astype(np.float32)[:, feature // 2].T
    sin = np.sin(angle).astype(np.float32)[:, feature // 2].T * np.where(feature % 2, 1.0, -1.0)[:, None]
    c["rot"] = np.stack([cos, sin], 1).astype(np.float32)
    row = np.arange(P)
    q, b, e = row // 32, row // 16 % 2, row % 16
    same = (b[:, None] == b) & (e[:, None] == e)
    c["blocksum"] = same.astype(np.float32)
    c["before"] = (same & (q[:, None] < q)).astype(np.float32)
    c["rank"] = np.broadcast_to(np.arange(NE1, 0, -1, dtype=np.float32), (P, 1, NE1)).copy()
    unit = np.arange(P)
    spread = (q[:, None, None, None, None] == np.arange(QC)[:, None, None, None]) & (
        b[:, None, None, None, None] == np.arange(B)[:, None, None]) & (
        e[:, None, None, None, None] == (np.arange(FC1)[:, None] * (P // F1) + unit // F1))
    c["spread"] = spread.astype(half_type)
    return c


def layouts(i):
    a = {"x": i["L0_attn_x"]}
    cols = np.arange(E).reshape(GB, HG, D).transpose(0, 2, 1).ravel()
    swap = np.arange(E) ^ 1
    for L in range(2):
        if L == 0:
            w, bias, wp, bp = i["L0_attn_Wqkv"], i["L0_attn_bqkv"], i["L0_attn_Wproj"], i["L0_attn_bproj"]
        else:
            w, bias, wp, bp = i["L1_attn_w_qkv"].T, i["L1_attn_b_qkv"], i["L1_attn_w_out"].T, i["L1_attn_b_out"]
        q, k, v = w[:, :E], w[:, E:2 * E], w[:, 2 * E:]
        bq, bk, bv = bias[:E], bias[E:2 * E], bias[2 * E:]
        a[f"wqk{L}"] = np.stack([q[:, cols], q[:, swap[cols]], k[:, cols], k[:, swap[cols]]], 1)
        a[f"bqk{L}"] = np.stack([bq[cols], bq[swap[cols]], bk[cols], bk[swap[cols]]], 1)
        a[f"wv{L}"], a[f"wp{L}"] = v, wp
        a[f"bvb{L}"] = np.broadcast_to(bv, (P, E))
        a[f"bpb{L}"] = np.broadcast_to(bp, (P, E))
    a["slot_emb"] = i["L0_ffn_slot_embeds"].reshape(NB0, P, E).transpose(1, 0, 2)
    gam = np.stack([i["L0_ffn_norm_gamma"], i["L0_ffn_slot_norm_gamma"]])
    a["gam0"] = np.broadcast_to(gam, (P, 2, E))
    a["w1_0"] = i["L0_ffn_w1"].transpose(1, 0, 2)
    a["w2_0"] = i["L0_ffn_w2"].reshape(NE0, HC0, P, E).transpose(2, 0, 1, 3)
    a["b1_0"] = i["L0_ffn_b1"].reshape(NE0, HC0, P).transpose(2, 0, 1)
    b2 = i["L0_ffn_b2"].reshape(NB0, 2, E)
    a["b2_0"] = np.repeat(b2, SL0, axis=1).transpose(1, 0, 2)
    a["wg"] = i["L1_ffn_wg"]
    a["bgb"] = np.broadcast_to(i["L1_ffn_bg"], (P, NE1))
    a["rw1"] = i["L1_ffn_w1"].transpose(1, 0, 2).reshape(E, NE1 * F1)
    a["rw2"] = i["L1_ffn_w2"].reshape(FC1, P, E).transpose(1, 0, 2)
    a["rb1"] = i["L1_ffn_b1"].reshape(FC1, P).T
    rb2 = np.zeros((QC, B, NE1, QC, B, E), np.float32)
    for q in range(QC):
        for b in range(B):
            rb2[q, b, :, q, b, :] = i["L1_ffn_b2"]
    a["rb2"] = rb2.reshape(P, QC, B, E)
    a["gam1"] = np.broadcast_to(i["L1_ffn_gamma"], (P, E))
    a["bet1"] = np.broadcast_to(i["L1_ffn_beta"], (P, E))
    return a


def kernel(**inputs):
    from concourse import bacc
    from concourse.bass_utils import run_bass_kernel_spmd

    nc = bacc.Bacc("TRN2", target_bir_lowering=False, num_devices=1)
    arrays = layouts({k: np.asarray(v) for k, v in inputs.items()})
    arrays.update(constants())
    arrays = {f"in_{k}": np.ascontiguousarray(v) for k, v in arrays.items()}
    a = {k[3:]: nc.dram_tensor(k, v.shape, mybir.dt.from_np(v.dtype), kind="ExternalInput").ap()
         for k, v in arrays.items()}
    out = nc.dram_tensor("out", (B, T, E), F32, kind="ExternalOutput").ap()
    block_kernel(nc, a, out)
    r = run_bass_kernel_spmd(nc, [arrays], core_ids=[0])
    return r.results[0]["out"]
```
